# Optimizing a Trainium2 kernel written in Bass

```python
import numpy as np
import jax
import jax.numpy as jnp

def _softmax(x, axis=-1):
    return jax.nn.softmax(x, axis=axis)

def _gelu(x):
    return jax.nn.gelu(x, approximate=True)

def _silu(x):
    return jax.nn.silu(x)

def _sigmoid(x):
    return jax.nn.sigmoid(x)

def _layernorm(x, axis=-1, eps=1e-05):
    m = jnp.mean(x, axis=axis, keepdims=True)
    v = jnp.var(x, axis=axis, keepdims=True)
    return (x - m) / jnp.sqrt(v + eps)

def _scatter_add(tgt, idx, src, axis=0):
    return tgt.at[idx].add(src)

def _segment_sum(src, seg, n):
    return jax.ops.segment_sum(src, seg, n)
kernel_name = 'mk_dlrm_tower_d1_rec_r8_40f16d'

def setup_inputs(seed: int=0):
    np.random.seed(seed)
    _w = jnp.asarray

    def _rec_inputs():
        import jax
        import jax.numpy as jnp
        _tk = jax.random.key(seed)
        ids = jnp.stack([jax.random.randint(jax.random.fold_in(_tk, 200 + f), (512,), 0, v, jnp.int32) for f, v in enumerate([1000, 12500, 1250, 1000, 125000, 1250, 12500, 1000, 1000, 1250, 1250, 12500, 1250, 1000, 12500, 1250, 1250, 1000, 12500, 1000, 1250, 1250, 12500, 1250, 12500, 12500])], axis=1)
        tbl_0 = 0.05 * jax.random.normal(jax.random.fold_in(_tk, 500 + 0), (1000, 128), jnp.float32)
        tbl_1 = 0.05 * jax.random.normal(jax.random.fold_in(_tk, 500 + 1), (12500, 128), jnp.float32)
        tbl_2 = 0.05 * jax.random.normal(jax.random.fold_in(_tk, 500 + 2), (1250, 128), jnp.float32)
        tbl_3 = 0.05 * jax.random.normal(jax.random.fold_in(_tk, 500 + 3), (1000, 128), jnp.float32)
        tbl_4 = 0.05 * jax.random.normal(jax.random.fold_in(_tk, 500 + 4), (125000, 128), jnp.float32)
        tbl_5 = 0.05 * jax.random.normal(jax.random.fold_in(_tk, 500 + 5), (1250, 128), jnp.float32)
        tbl_6 = 0.05 * jax.random.normal(jax.random.fold_in(_tk, 500 + 6), (12500, 128), jnp.float32)
        tbl_7 = 0.05 * jax.random.normal(jax.random.fold_in(_tk, 500 + 7), (1000, 128), jnp.float32)
        tbl_8 = 0.05 * jax.random.normal(jax.random.fold_in(_tk, 500 + 8), (1000, 128), jnp.float32)
        tbl_9 = 0.05 * jax.random.normal(jax.random.fold_in(_tk, 500 + 9), (1250, 128), jnp.float32)
        tbl_10 = 0.05 * jax.random.normal(jax.random.fold_in(_tk, 500 + 10), (1250, 128), jnp.float32)
        tbl_11 = 0.05 * jax.random.normal(jax.random.fold_in(_tk, 500 + 11), (12500, 128), jnp.float32)
        tbl_12 = 0.05 * jax.random.normal(jax.random.fold_in(_tk, 500 + 12), (1250, 128), jnp.float32)
        tbl_13 = 0.05 * jax.random.normal(jax.random.fold_in(_tk, 500 + 13), (1000, 128), jnp.float32)
        tbl_14 = 0.05 * jax.random.normal(jax.random.fold_in(_tk, 500 + 14), (12500, 128), jnp.float32)
        tbl_15 = 0.05 * jax.random.normal(jax.random.fold_in(_tk, 500 + 15), (1250, 128), jnp.float32)
        tbl_16 = 0.05 * jax.random.normal(jax.random.fold_in(_tk, 500 + 16), (1250, 128), jnp.float32)
        tbl_17 = 0.05 * jax.random.normal(jax.random.fold_in(_tk, 500 + 17), (1000, 128), jnp.float32)
        tbl_18 = 0.05 * jax.random.normal(jax.random.fold_in(_tk, 500 + 18), (12500, 128), jnp.float32)
        tbl_19 = 0.05 * jax.random.normal(jax.random.fold_in(_tk, 500 + 19), (1000, 128), jnp.float32)
        tbl_20 = 0.05 * jax.random.normal(jax.random.fold_in(_tk, 500 + 20), (1250, 128), jnp.float32)
        tbl_21 = 0.05 * jax.random.normal(jax.random.fold_in(_tk, 500 + 21), (1250, 128), jnp.float32)
        tbl_22 = 0.05 * jax.random.normal(jax.random.fold_in(_tk, 500 + 22), (12500, 128), jnp.float32)
        tbl_23 = 0.05 * jax.random.normal(jax.random.fold_in(_tk, 500 + 23), (1250, 128), jnp.float32)
        tbl_24 = 0.05 * jax.random.normal(jax.random.fold_in(_tk, 500 + 24), (12500, 128), jnp.float32)
        tbl_25 = 0.05 * jax.random.normal(jax.random.fold_in(_tk, 500 + 25), (12500, 128), jnp.float32)
        _rk = jax.random.fold_in(_tk, 7)
        r_dense_output = -0.000520686 + 1.00062 * jax.random.normal(jax.random.fold_in(_rk, 101), (512, 128), jnp.float32)
        W_top1 = 0.0405887 * jax.random.normal(jax.random.fold_in(_tk, 801), (607, 512), jnp.float32)
        W_top2 = 0.0441942 * jax.random.normal(jax.random.fold_in(_tk, 802), (512, 256), jnp.float32)
        W_top3 = 0.0625 * jax.random.normal(jax.random.fold_in(_tk, 803), (256, 1), jnp.float32)
        b_top1 = jnp.zeros((512,), jnp.float32)
        b_top2 = jnp.zeros((256,), jnp.float32)
        return (r_dense_output, ids, tbl_0, tbl_1, tbl_2, tbl_3, tbl_4, tbl_5, tbl_6, tbl_7, tbl_8, tbl_9, tbl_10, tbl_11, tbl_12, tbl_13, tbl_14, tbl_15, tbl_16, tbl_17, tbl_18, tbl_19, tbl_20, tbl_21, tbl_22, tbl_23, tbl_24, tbl_25, W_top1, b_top1, W_top2, b_top2, W_top3)
    r_dense_output, ids, tbl_0, tbl_1, tbl_2, tbl_3, tbl_4, tbl_5, tbl_6, tbl_7, tbl_8, tbl_9, tbl_10, tbl_11, tbl_12, tbl_13, tbl_14, tbl_15, tbl_16, tbl_17, tbl_18, tbl_19, tbl_20, tbl_21, tbl_22, tbl_23, tbl_24, tbl_25, W_top1, b_top1, W_top2, b_top2, W_top3 = _rec_inputs()

    def _L0_rec_setup():
        import jax, jax.numpy as jnp
        import numpy as np
        B, NUM_SPARSE, D = (2048, 26, 128)
        key = jax.random.key(seed)
        k1, k2 = jax.random.split(key)
        dense_output = jax.random.normal(k1, (B, D), dtype=jnp.float32)
        embeddings = jax.random.normal(k2, (B, NUM_SPARSE, D), dtype=jnp.float32)
        return {'dense_output': dense_output, 'embeddings': embeddings}
    _L0_rec_all = _L0_rec_setup()
    _L0_rec_in = {k: v for k, v in _L0_rec_all.items() if k in ()}
    del _L0_rec_all
    return {'r_dense_output': r_dense_output, 'ids': ids, 'tbl_0': tbl_0, 'tbl_1': tbl_1, 'tbl_2': tbl_2, 'tbl_3': tbl_3, 'tbl_4': tbl_4, 'tbl_5': tbl_5, 'tbl_6': tbl_6, 'tbl_7': tbl_7, 'tbl_8': tbl_8, 'tbl_9': tbl_9, 'tbl_10': tbl_10, 'tbl_11': tbl_11, 'tbl_12': tbl_12, 'tbl_13': tbl_13, 'tbl_14': tbl_14, 'tbl_15': tbl_15, 'tbl_16': tbl_16, 'tbl_17': tbl_17, 'tbl_18': tbl_18, 'tbl_19': tbl_19, 'tbl_20': tbl_20, 'tbl_21': tbl_21, 'tbl_22': tbl_22, 'tbl_23': tbl_23, 'tbl_24': tbl_24, 'tbl_25': tbl_25, 'W_top1': W_top1, 'b_top1': b_top1, 'W_top2': W_top2, 'b_top2': b_top2, 'W_top3': W_top3}

def reference(r_dense_output, ids, tbl_0, tbl_1, tbl_2, tbl_3, tbl_4, tbl_5, tbl_6, tbl_7, tbl_8, tbl_9, tbl_10, tbl_11, tbl_12, tbl_13, tbl_14, tbl_15, tbl_16, tbl_17, tbl_18, tbl_19, tbl_20, tbl_21, tbl_22, tbl_23, tbl_24, tbl_25, W_top1, b_top1, W_top2, b_top2, W_top3):
    import jax
    import jax.numpy as jnp

    def _L0_rec_ref(dense_output, embeddings):
        import jax, jax.numpy as jnp
        import numpy as np
        B, NUM_SPARSE, D = (2048, 26, 128)
        combined = jnp.concatenate([dense_output[:, None, :], embeddings], axis=1)
        interactions = jnp.einsum('bfd,bgd->bfg', combined, combined)
        F = combined.shape[1]
        iu, ju = jnp.triu_indices(F, k=1)
        interactions_flat = interactions[:, iu, ju]
        return jnp.concatenate([dense_output, interactions_flat], axis=1)
    e = jnp.stack([tbl_0[ids[:, 0]], tbl_1[ids[:, 1]], tbl_2[ids[:, 2]], tbl_3[ids[:, 3]], tbl_4[ids[:, 4]], tbl_5[ids[:, 5]], tbl_6[ids[:, 6]], tbl_7[ids[:, 7]], tbl_8[ids[:, 8]], tbl_9[ids[:, 9]], tbl_10[ids[:, 10]], tbl_11[ids[:, 11]], tbl_12[ids[:, 12]], tbl_13[ids[:, 13]], tbl_14[ids[:, 14]], tbl_15[ids[:, 15]], tbl_16[ids[:, 16]], tbl_17[ids[:, 17]], tbl_18[ids[:, 18]], tbl_19[ids[:, 19]], tbl_20[ids[:, 20]], tbl_21[ids[:, 21]], tbl_22[ids[:, 22]], tbl_23[ids[:, 23]], tbl_24[ids[:, 24]], tbl_25[ids[:, 25]]], axis=1)
    z = _L0_rec_ref(r_dense_output, e)
    z = z.reshape(z.shape[0], -1)
    h = jnp.concatenate([z, r_dense_output], axis=1)
    h = jnp.maximum(h @ W_top1 + b_top1, 0.0)
    h = jnp.maximum(h @ W_top2 + b_top2, 0.0)
    y = h @ W_top3
    return y

_drawn_inputs = setup_inputs


def setup_inputs(seed=0):
    import zlib

    import numpy as np

    out = dict(_drawn_inputs(seed))
    spreads = {'b_top1': (0.0, 0.1), 'b_top2': (0.0, 0.1)}
    factors = {}
    for name, (base, spread) in spreads.items():
        noise = np.random.default_rng([zlib.crc32(name.encode()), seed]).standard_normal(out[name].shape)
        drawn = base * np.exp(spread * noise) if base else spread * noise
        out[name] = jnp.asarray(drawn.astype(out[name].dtype))
    for name, factor in factors.items():
        out[name] = (out[name] * factor).astype(out[name].dtype)
    return out
```

```python
from contextlib import ExitStack

import concourse.bass as bass
from concourse import mybir

F32 = mybir.dt.float32
F32R = mybir.dt.float32r
I32 = mybir.dt.int32
ALU = mybir.AluOpType
ACT = mybir.ActivationFunctionType

P = 128
D = 128
BATCH = 512
TILES = BATCH // P
ROWS = [1000, 12500, 1250, 1000, 125000, 1250, 12500, 1000, 1000, 1250, 1250, 12500, 1250, 1000, 12500, 1250, 1250,
        1000, 12500, 1000, 1250, 1250, 12500, 1250, 12500, 12500]
TABLES = len(ROWS)
SLOTS = 32
USED = TABLES + 1
H1, H2 = 512, 256

ONEHOT = [0, 3, 7, 8, 13, 17, 19, 2]
GATHERED = [f for f in range(TABLES) if f not in ONEHOT]
NHOT = len(ONEHOT)
TP = 125
DEPTH = [ROWS[f] // TP for f in ONEHOT]
MAXDEPTH = max(DEPTH)
HOT_BEFORE = [sum(DEPTH[:j]) for j in range(NHOT + 1)]
SLOT_FEATURE = [0] + [1 + f for f in ONEHOT] + [1 + f for f in GATHERED]

QUAD = 4
ROW_UNITS = [range(q, min(q + QUAD, len(GATHERED))) for q in range(0, len(GATHERED), QUAD)]
NU = len(ROW_UNITS)

GROUPS = P // QUAD
HALF = GROUPS // 2
GCOLS = USED - 1

PAIRS = USED * (USED - 1) // 2
KT = 3
KP = PAIRS // KT

RAW_RING, SPLIT_RING, IDS_RING, HOT_RING, X_RING = 3, 2, 3, 6, 2


def packed_blocks():
    half, b = 14, 7
    blocks = [((g0, 1, ng), (f0, 0, nf)) for g0, ng, f0, nf in
              [(half, USED - half, 0, half), (b, b, 0, b), (3 * b, USED - 3 * b, half, b)]]
    for r in range(1, b):
        m = sum(1 for i in range(4) if i * b + r < USED)
        blocks.append(((r, b, m), (0, b, r)))
    return blocks


def packed_pairs():
    return [(g0 + i * gs, f0 + i * fs + j)
            for (g0, gs, ng), (f0, fs, nf) in packed_blocks() for i in range(ng) for j in range(nf)]


def schedule():
    hot = [("hot", j, 0) for j in range(NHOT)]
    rows = [[("rows", t, u) for u in range(NU)] for t in range(TILES)]
    steps = hot[:6] + rows[0] + hot[6:] + [("gram", 0, 0)] + rows[1]
    for t in range(TILES):
        if t >= 1:
            steps += [("l2", t - 1, 0)]
        steps += [("pairs", t, 0)]
        if t >= 1:
            steps += [("l3", t - 1, 0)]
        if t + 1 < TILES:
            steps += [("gram", t + 1, 0)]
        steps += [("l1", t, 0)]
        if t + 2 < TILES:
            steps += rows[t + 2]
    steps += [("l2", TILES - 1, 0), ("l3", TILES - 1, 0)]
    return steps


STEPS = schedule()
X_UNITS = [s for s in STEPS if s[0] in ("hot", "rows")]
X_INDEX = {s: n for n, s in enumerate(X_UNITS)}


def x_units_of(t):
    return 1 + max(n for n, (kind, a, _) in enumerate(X_UNITS) if kind == "hot" or a == t)


def build(nc, gather_ids, hot_ids, consts, tables, dense_t, w_dense, w_dense2, w_pairs, b1, w2, b2, w3, out):
    with ExitStack() as ctx:
        def sb(name, shape, dt=F32):
            return ctx.enter_context(nc.sbuf_tensor(name, shape, dt))

        def psum(name, shape, dt=F32):
            return ctx.enter_context(nc.psum_tensor(name, shape, dt))

        def sem(name):
            return ctx.enter_context(nc.semaphore(name))

        idx = sb("idx", [P, TILES, len(GATHERED)], I32)
        cst = sb("cst", [P, P + 2 * MAXDEPTH])
        ident = cst[:, 0:P]
        row_number = {1000: cst[0:TP, P:P + MAXDEPTH], 1250: cst[0:TP, P + MAXDEPTH:P + 2 * MAXDEPTH]}
        rows = sb("rows", [P, TILES, len(GATHERED), D])
        raw = sb("raw", [TP, RAW_RING, MAXDEPTH, D])
        hi = sb("hi", [TP, SPLIT_RING, MAXDEPTH, D], F32R)
        lo = sb("lo", [TP, SPLIT_RING, MAXDEPTH, D], F32R)
        ids_b = sb("ids_b", [TP, IDS_RING, BATCH], I32)
        hot = sb("hot", [TP, HOT_RING, BATCH], F32R)
        dense = sb("dense", [P, BATCH])
        x_t = sb("x_t", [P, BATCH, SLOTS])
        PW = 4 * 7 * (SLOTS + 1)
        prod_b = sb("prod_b", [P, PW])
        packed = sb("packed", [P, 2, PAIRS])
        z_t = sb("z_t", [P, KT, P])
        wd = sb("wd", [P, H1])
        wd2 = sb("wd2", [P, H1])
        wds = sb("wds", [P, H1])
        wp = sb("wp", [P, KT, H1])
        w2s = sb("w2s", [P, H1 // P, H2])
        w3s = sb("w3s", [P, H2 // P])
        b2s = sb("b2s", [P, H2 // P])
        h1 = sb("h1", [P, H1])
        h2 = sb("h2", [P, H2])
        y = sb("y", [1, BATCH])

        ps_x = [psum(f"ps_x{i}", [P, BATCH]) for i in range(X_RING)]
        ps_gb = [psum(f"ps_g{i}", [P, 2, 512]) for i in range(2)]
        ps_g = [b[:, :, 0:HALF * GCOLS].rearrange("p h (i g) -> p h i g", g=GCOLS) for b in ps_gb]
        ps_l23 = psum("ps_l23", [P, 512])
        ps_l1 = psum("ps_l1", [P, H1])

        idx_in = sem("idx_in")
        cst_in = sem("cst_in")
        raw_in = [sem(f"raw_in{i}") for i in range(RAW_RING)]
        ids_in = [sem(f"ids_in{i}") for i in range(IDS_RING)]
        dense_in = sem("dense_in")
        wd_in = sem("wd_in")
        wp_in = sem("wp_in")
        w2_in = sem("w2_in")
        rows_in = [[sem(f"rows_in{t}_{u}") for u in range(NU)] for t in range(TILES)]
        pad_set = sem("pad_set")
        dense_set = sem("dense_set")
        ones_set = sem("ones_set")
        wd_summed = sem("wd_summed")
        hi_ready = sem("hi_ready")
        lo_ready = sem("lo_ready")
        hot_ready = sem("hot_ready")
        hot_used = sem("hot_used")
        x_ready = sem("x_ready")
        x_copied = sem("x_copied")
        gram_ready = sem("gram_ready")
        turned = sem("turned")
        pairs_packed = sem("pairs_packed")
        pairs_turned = sem("pairs_turned")
        z_ready = sem("z_ready")
        l1_ready = sem("l1_ready")
        h1_ready = sem("h1_ready")
        l2_ready = sem("l2_ready")
        h2_ready = sem("h2_ready")
        l3_ready = sem("l3_ready")
        y_ready = sem("y_ready")
        out_done = sem("out_done")

        NBLOCKS = len(packed_blocks())
        block = ctx.enter_context(nc.Block())

        @block.sync
        def _(sp):
            sp.dma_start(idx[:], gather_ids).then_inc(idx_in, 16)
            sp.dma_start(cst[:], consts).then_inc(cst_in, 16)
            for j in range(NHOT):
                if j >= IDS_RING:
                    sp.wait_ge(hot_ready, HOT_BEFORE[j - IDS_RING + 1])
                sp.dma_start(ids_b[:, j % IDS_RING, :],
                             hot_ids[j:j + 1, :].to_broadcast([TP, BATCH])).then_inc(ids_in[j % IDS_RING], 16)
                if j >= RAW_RING:
                    sp.wait_ge(lo_ready, j - RAW_RING + 1)
                sp.dma_start(raw[:, j % RAW_RING, 0:DEPTH[j], :],
                             tables[ONEHOT[j]].rearrange("(p k) d -> p k d", p=TP)).then_inc(raw_in[j % RAW_RING], 16)
                if j == 0:
                    sp.dma_start(dense[:], dense_t).then_inc(dense_in, 16)
                if j == RAW_RING:
                    sp.dma_start(wd[:], w_dense).then_inc(wd_in, 16)
                    sp.dma_start(wd2[:], w_dense2).then_inc(wd_in, 16)
                    sp.dma_start(wp[0:KP, :, :], w_pairs.rearrange("(k p) n -> p k n", p=KP)).then_inc(wp_in, 16)
                    sp.dma_start(wp[KP:KP + 1, KT - 1, :], b1).then_inc(wp_in, 16)
                    sp.dma_start(w2s[:], w2.rearrange("(k p) n -> p k n", p=P)).then_inc(w2_in, 16)
                    sp.dma_start(w3s[:], w3).then_inc(w2_in, 16)
                    sp.dma_start(b2s[:], b2).then_inc(w2_in, 16)
            sp.wait_ge(y_ready, TILES)
            sp.dma_start(out, y[:]).then_inc(out_done, 16)
            sp.wait_ge(out_done, 16)

        @block.gpsimd
        def _(pool):
            pool.wait_ge(idx_in, 16)
            for t in range(TILES):
                for u in range(NU):
                    for g in ROW_UNITS[u]:
                        pool.indirect_dma_start(rows[:, t, g, :], None, tables[GATHERED[g]],
                                                bass.IndirectOffsetOnAxis(idx[:, t, g:g + 1], 0)
                                                ).then_inc(rows_in[t][u], 16)

        @block.tensor
        def _(pe):
            def x_bank(unit):
                n = X_INDEX[unit]
                if n >= X_RING:
                    pe.wait_ge(x_copied, n - X_RING + 1)
                return ps_x[n % X_RING]

            def hot_rows(j):
                bank = x_bank(("hot", j, 0))
                pe.wait_ge(hi_ready, j + 1)
                pe.wait_ge(lo_ready, j + 1)
                for k in range(DEPTH[j]):
                    n = HOT_BEFORE[j] + k
                    pe.wait_ge(hot_ready, n + 1)
                    pe.matmul(bank[:], hi[:, j % SPLIT_RING, k, :], hot[:, n % HOT_RING, :],
                              start=(k == 0), stop=False)
                    last = pe.matmul(bank[:], lo[:, j % SPLIT_RING, k, :], hot[:, n % HOT_RING, :],
                                     start=False, stop=(k == DEPTH[j] - 1))
                    if k < DEPTH[j] - 1:
                        last.then_inc(hot_used, 1)
                    else:
                        last.then_inc(x_ready, 1)

            def gathered_rows(t, u):
                bank = x_bank(("rows", t, u))
                pe.wait_ge(cst_in, 16)
                pe.wait_ge(rows_in[t][u], 16 * len(ROW_UNITS[u]))
                for i, g in enumerate(ROW_UNITS[u]):
                    last = pe.transpose(bank[:, i * P:(i + 1) * P], rows[:, t, g, :], ident)
                last.then_inc(x_ready, 1)

            def gram(t):
                pe.wait_ge(x_copied, x_units_of(t))
                if t == 0:
                    pe.wait_ge(pad_set, 1)
                    pe.wait_ge(dense_set, 1)
                x = x_t[:, t * P:(t + 1) * P, :].rearrange("d (i q) s -> d i q s", q=QUAD)
                if t >= 2:
                    pe.wait_ge(turned, t - 1)
                for i in range(GROUPS):
                    for q in range(QUAD):
                        last = pe.matmul(ps_g[t % 2][q * SLOTS:(q + 1) * SLOTS, i // HALF, i % HALF, :],
                                         x[:, i, q, :], x[:, i, q, 1:USED], start=True, stop=True)
                last.then_inc(gram_ready, 1)

            def turn_pairs(t):
                pe.wait_ge(pairs_packed, NBLOCKS * (t + 1))
                if t >= 1:
                    pe.wait_ge(h1_ready, t)
                for k in range(KT):
                    last = pe.transpose(ps_l1[0:KP, k * P:(k + 1) * P], packed[:, t % 2, k * KP:(k + 1) * KP], ident)
                last.then_inc(pairs_turned, 1)

            def layer1(t):
                if t == 0:
                    pe.wait_ge(wd_summed, 1)
                    pe.wait_ge(wp_in, 32)
                    pe.wait_ge(ones_set, 1)
                pe.wait_ge(z_ready, t + 1)
                for n in range(H1 // P):
                    o = ps_l1[:, n * P:(n + 1) * P]
                    pe.matmul(o, wds[:, n * P:(n + 1) * P], dense[:, t * P:(t + 1) * P], start=True, stop=False)
                    for k in range(KT):
                        kp = KP + (k == KT - 1)
                        last = pe.matmul(o, wp[0:kp, k, n * P:(n + 1) * P], z_t[0:kp, k, :],
                                         start=False, stop=(k == KT - 1))
                last.then_inc(l1_ready, 1)

            def layer2(t):
                if t == 0:
                    pe.wait_ge(w2_in, 48)
                else:
                    pe.wait_ge(y_ready, t)
                pe.wait_ge(h1_ready, t + 1)
                for n in range(H2 // P):
                    for k in range(H1 // P):
                        last = pe.matmul(ps_l23[:, n * P:(n + 1) * P], w2s[:, k, n * P:(n + 1) * P],
                                         h1[:, k * P:(k + 1) * P], start=(k == 0), stop=(k == H1 // P - 1))
                last.then_inc(l2_ready, 1)

            def layer3(t):
                pe.wait_ge(h2_ready, (H2 // P) * (t + 1))
                for k in range(H2 // P):
                    last = pe.matmul(ps_l23[0:1, 384:384 + P], w3s[:, k:k + 1], h2[:, k * P:(k + 1) * P],
                                     start=(k == 0), stop=(k == H2 // P - 1))
                last.then_inc(l3_ready, 1)

            for kind, a, u in STEPS:
                if kind == "hot":
                    hot_rows(a)
                elif kind == "rows":
                    gathered_rows(a, u)
                else:
                    {"gram": gram, "pairs": turn_pairs, "l1": layer1, "l2": layer2, "l3": layer3}[kind](a)

        @block.scalar
        def _(act):
            def high_part(j):
                act.wait_ge(raw_in[j % RAW_RING], 16 * (j // RAW_RING + 1))
                if j >= SPLIT_RING:
                    act.wait_ge(x_ready, X_INDEX[("hot", j - SPLIT_RING, 0)] + 1)
                act.activation(hi[:, j % SPLIT_RING, 0:DEPTH[j], :], raw[:, j % RAW_RING, 0:DEPTH[j], :],
                               ACT.Copy).then_inc(hi_ready, 1)

            def copy_x(unit):
                n = X_INDEX[unit]
                kind, a, u = unit
                act.wait_ge(x_ready, n + 1)
                if kind == "hot":
                    act.activation(x_t[:, :, 1 + a], ps_x[n % X_RING][:], ACT.Copy).then_inc(x_copied, 1)
                else:
                    g = ROW_UNITS[u]
                    act.activation(x_t[:, a * P:(a + 1) * P, 1 + NHOT + g[0]:1 + NHOT + g[-1] + 1],
                                   ps_x[n % X_RING][:, 0:len(g) * P].rearrange("d (s b) -> d b s", b=P),
                                   ACT.Copy).then_inc(x_copied, 1)

            def relu1(t):
                act.wait_ge(l1_ready, t + 1)
                if t >= 1:
                    act.wait_ge(l2_ready, t)
                act.activation(h1[:], ps_l1[:], ACT.Relu).then_inc(h1_ready, 1)

            def relu2(t):
                act.wait_ge(l2_ready, t + 1)
                if t == 0:
                    act.wait_ge(w2_in, 48)
                if t >= 1:
                    act.wait_ge(l3_ready, t)
                for n in range(H2 // P):
                    act.activation(h2[:, n * P:(n + 1) * P], ps_l23[:, n * P:(n + 1) * P], ACT.Relu,
                                   bias=b2s[:, n:n + 1]).then_inc(h2_ready, 1)

            high_part(0)
            high_part(1)
            for step in STEPS:
                kind, a, u = step
                if kind in ("hot", "rows"):
                    copy_x(step)
                    if kind == "hot" and a + 2 < NHOT:
                        high_part(a + 2)
                elif kind == "l1":
                    relu1(a)
                elif kind == "l2":
                    relu2(a)

        @block.vector
        def _(dve):
            def low_part(j):
                dve.wait_ge(hi_ready, j + 1)
                dve.tensor_tensor(lo[:, j % SPLIT_RING, 0:DEPTH[j], :], raw[:, j % RAW_RING, 0:DEPTH[j], :],
                                  hi[:, j % SPLIT_RING, 0:DEPTH[j], :].bitcast(F32),
                                  ALU.subtract).then_inc(lo_ready, 1)

            def one_hot(j):
                dve.wait_ge(ids_in[j % IDS_RING], 16 * (j // IDS_RING + 1))
                for k in range(DEPTH[j]):
                    n = HOT_BEFORE[j] + k
                    m = n - HOT_RING
                    if m >= 0:
                        jm = max(i for i in range(NHOT) if HOT_BEFORE[i] <= m)
                        km = m - HOT_BEFORE[jm]
                        if km < DEPTH[jm] - 1:
                            dve.wait_ge(hot_used, m - jm + 1)
                        else:
                            dve.wait_ge(x_ready, X_INDEX[("hot", jm, 0)] + 1)
                    dve.tensor_scalar(hot[:, n % HOT_RING, :], ids_b[:, j % IDS_RING, :],
                                      row_number[ROWS[ONEHOT[j]]][:, k:k + 1], None,
                                      ALU.is_equal).then_inc(hot_ready, 1)

            def turn_gram(t):
                dve.wait_ge(gram_ready, t + 1)
                if t >= 1:
                    dve.wait_ge(pairs_packed, NBLOCKS * t)
                dve.transpose(prod_b[:, 0:GCOLS * SLOTS], ps_g[t % 2].rearrange("p h i g -> p g h i")
                              ).then_inc(turned, 1)
                dve.wait_ge(turned, t + 1)
                if t >= 2:
                    dve.wait_ge(pairs_turned, t - 1)
                at = 0
                for (g0, gs, ng), (f0, fs, nf) in packed_blocks():
                    step = gs * SLOTS + fs
                    first = (g0 - 1) * SLOTS + f0
                    base = first // step * step if step > SLOTS else first - first % SLOTS
                    v = prod_b[:, base:base + ng * step].rearrange("p (m s) -> p m s", s=step)
                    o = packed[:, t % 2, at:at + ng * nf].rearrange("p (m s) -> p m s", s=nf)
                    dve.tensor_copy(o, v[:, :, first - base:first - base + nf]).then_inc(pairs_packed, 1)
                    at += ng * nf

            def copy_z(t):
                dve.wait_ge(pairs_turned, t + 1)
                if t >= 1:
                    dve.wait_ge(l1_ready, t)
                dve.tensor_copy(z_t[0:KP, :, :], ps_l1[0:KP, 0:KT * P].rearrange("p (k b) -> p k b", b=P)
                                ).then_inc(z_ready, 1)

            def copy_y(t):
                dve.wait_ge(l3_ready, t + 1)
                dve.tensor_copy(y[:, t * P:(t + 1) * P], ps_l23[0:1, 384:384 + P]).then_inc(y_ready, 1)

            dve.memset(z_t[96:P, KT - 1, :], 1.0).then_inc(ones_set, 1)
            dve.memset(x_t[:, :, USED:SLOTS], 0.0).then_inc(pad_set, 1)
            dve.wait_ge(cst_in, 16)
            dve.wait_ge(ones_set, 1)
            for j in range(NHOT):
                low_part(j)
                one_hot(j)
                if j == 0:
                    dve.wait_ge(dense_in, 16)
                    dve.tensor_copy(x_t[:, :, 0].rearrange("d (t i q) -> d t i q", t=TILES, q=QUAD),
                                    dense[:].rearrange("d (t q i) -> d t i q", t=TILES, q=QUAD)
                                    ).then_inc(dense_set, 1)
            dve.wait_ge(wd_in, 32)
            dve.tensor_tensor(wds[:], wd[:], wd2[:], ALU.add).then_inc(wd_summed, 1)
            for kind, a, _ in STEPS:
                if kind == "gram":
                    turn_gram(a)
                elif kind == "pairs":
                    copy_z(a)
                elif kind == "l3":
                    copy_y(a)


def kernel(**inputs):
    import numpy as np
    import concourse.bacc as bacc
    from concourse import mybir as mb
    from concourse.bass_utils import run_bass_kernel_spmd as run

    nc = bacc.Bacc("TRN2", target_bir_lowering=False, num_devices=1)
    ids = np.ascontiguousarray(inputs["ids"])
    w1 = np.ascontiguousarray(inputs["W_top1"])
    number = {}
    for f in range(USED):
        for g in range(f + 1, USED):
            number[f, g] = D + len(number)
    order = [number[tuple(sorted((SLOT_FEATURE[g], SLOT_FEATURE[f])))] for g, f in packed_pairs()]
    consts = np.zeros((P, P + 2 * MAXDEPTH), np.float32)
    consts[:, 0:P] = np.eye(P, dtype=np.float32)
    for i, depth in enumerate((8, 10)):
        for p in range(TP):
            for k in range(depth):
                consts[p, P + i * MAXDEPTH + k] = p * depth + k
    placed = ids.reshape(TILES, QUAD, GROUPS, TABLES).transpose(0, 2, 1, 3).reshape(BATCH, TABLES)
    data = {
        "gather_ids": placed[:, GATHERED].reshape(TILES, P, len(GATHERED)).transpose(1, 0, 2),
        "hot_ids": placed[:, ONEHOT].T,
        "consts": consts,
        "dense_t": np.asarray(inputs["r_dense_output"]).T,
        "w_dense": w1[0:D],
        "w_dense2": w1[D + PAIRS:],
        "w_pairs": w1[order],
        "b1": np.asarray(inputs["b_top1"]).reshape(1, H1),
        "w2": inputs["W_top2"],
        "b2": np.asarray(inputs["b_top2"]).reshape(H2 // P, P).T,
        "w3": np.asarray(inputs["W_top3"]).reshape(H2 // P, P).T,
    }
    for f in range(TABLES):
        data[f"tbl_{f}"] = inputs[f"tbl_{f}"]
    arrays, ap = {}, {}
    for name, a in data.items():
        a = np.ascontiguousarray(a)
        arrays[f"in_{name}"] = a
        ap[name] = nc.dram_tensor(f"in_{name}", a.shape, mb.dt.from_np(a.dtype), kind="ExternalInput").ap()
    o = nc.dram_tensor("out_0", (1, BATCH), mb.dt.float32, kind="ExternalOutput").ap()
    build(nc, ap["gather_ids"], ap["hot_ids"], ap["consts"], [ap[f"tbl_{f}"] for f in range(TABLES)], ap["dense_t"],
          ap["w_dense"], ap["w_dense2"], ap["w_pairs"], ap["b1"], ap["w2"], ap["b2"], ap["w3"], o)
    r = run(nc, [arrays], core_ids=[0])
    return r.results[0]["out_0"].reshape(BATCH, 1)
```

```python
from contextlib import ExitStack

import concourse.bass as bass
from concourse import mybir

F32 = mybir.dt.float32
F32R = mybir.dt.float32r
BF16 = mybir.dt.bfloat16
I32 = mybir.dt.int32
ALU = mybir.AluOpType
ACT = mybir.ActivationFunctionType

P = 128
D = 128
BATCH = 512
TILES = BATCH // P
ROWS = [1000, 12500, 1250, 1000, 125000, 1250, 12500, 1000, 1000, 1250, 1250, 12500, 1250, 1000, 12500, 1250, 1250,
        1000, 12500, 1000, 1250, 1250, 12500, 1250, 12500, 12500]
TABLES = len(ROWS)
SLOTS = 32
USED = TABLES + 1
H1, H2 = 512, 256

ONEHOT = [0, 3, 7, 8, 13, 17, 19, 2]
GATHERED = [f for f in range(TABLES) if f not in ONEHOT]
NHOT = len(ONEHOT)
TP = 125
DEPTH = [ROWS[f] // TP for f in ONEHOT]
DEPTHS = (8, 10)
MAXDEPTH = max(DEPTHS)
BY_SCALAR = 1
HOT_BEFORE = [sum(d - BY_SCALAR for d in DEPTH[:j]) for j in range(NHOT + 1)]
SLOT_FEATURE = [0] + [1 + f for f in ONEHOT] + [1 + f for f in GATHERED]

QUAD = 4
ROW_UNITS = [range(q, min(q + QUAD, len(GATHERED))) for q in range(0, len(GATHERED), QUAD)]
NU = len(ROW_UNITS)

GROUPS = P // QUAD
CHUNK = 8
CHUNKS = GROUPS // CHUNK
PITCH = 128
GCOLS = USED - 1

PAIRS = USED * (USED - 1) // 2
KT = 3
KP = PAIRS // KT

WARM_UP = 16
RAW_RING, SPLIT_RING, IDS_RING, HOT_RING, X_RING = 3, 2, 3, 6, 4


def packed_blocks():
    half, b = 14, 7
    blocks = [((g0, 1, ng), (f0, 0, nf)) for g0, ng, f0, nf in
              [(half, USED - half, 0, half), (b, b, 0, b), (3 * b, USED - 3 * b, half, b)]]
    for r in range(1, b):
        m = sum(1 for i in range(4) if i * b + r < USED)
        blocks.append(((r, b, m), (0, b, r)))
    return blocks


def packed_pairs():
    return [(g0 + i * gs, f0 + i * fs + j)
            for (g0, gs, ng), (f0, fs, nf) in packed_blocks() for i in range(ng) for j in range(nf)]


def schedule():
    rows = [[("rows", t, u) for u in range(NU)] for t in range(TILES)]
    early = rows[0] + rows[1][:NHOT - 1 - NU]
    steps = [("hot", 0, 0)]
    for j in range(1, NHOT):
        steps += [("hot", j, 0), early[j - 1]]
    steps += rows[1][NHOT - 1 - NU:] + [("gram", 0, 0)]
    for t in range(TILES):
        steps += [("pairs", t, 0)]
        if t >= 1:
            steps += [("l2", t - 1, 0)]
        if t + 1 < TILES:
            steps += [("gram", t + 1, 0)]
        steps += [("l1", t, 0)]
        if t >= 1:
            steps += [("l3", t - 1, 0)]
        if t + 2 < TILES:
            steps += rows[t + 2]
    steps += [("l2", TILES - 1, 0), ("l3", TILES - 1, 0)]
    return steps


STEPS = schedule()
X_UNITS = [s for s in STEPS if s[0] in ("hot", "rows")]
X_INDEX = {s: n for n, s in enumerate(X_UNITS)}
BY_VECTOR = [n >= 2 * NHOT - 1 and n % 2 == 1 for n in range(len(X_UNITS))]


def copies(n, by_vector):
    return BY_VECTOR[:n].count(by_vector)


def units_before(step):
    before = STEPS[:STEPS.index(step)]
    return len([s for s in before if s in X_INDEX]), len([s for s in before if s[0] == "gram"])


def build(nc, gather_ids, hot_ids, consts, tables, dense_t, w_dense, w_dense2, w_pairs, b1, w2, b2, w3, out):
    with ExitStack() as ctx:
        def sb(name, shape, dt=F32):
            return ctx.enter_context(nc.sbuf_tensor(name, shape, dt))

        def psum(name, shape, dt=F32):
            return ctx.enter_context(nc.psum_tensor(name, shape, dt))

        def sem(name):
            return ctx.enter_context(nc.semaphore(name))

        idx = sb("idx", [P, TILES, len(GATHERED)], I32)
        ident_s = sb("ident", [P, P])
        ident = ident_s[:]
        numbers = sb("numbers", [TP, 4 * MAXDEPTH])
        row_number, minus_row_number = [
            {d: numbers[:, (i + s) * MAXDEPTH:(i + s + 1) * MAXDEPTH] for i, d in enumerate(DEPTHS)} for s in (0, 2)]
        rows = sb("rows", [P, TILES, len(GATHERED), D])
        raw = sb("raw", [TP, RAW_RING, MAXDEPTH, D])
        hi = sb("hi", [TP, SPLIT_RING, MAXDEPTH, D], F32R)
        lo = sb("lo", [TP, SPLIT_RING, MAXDEPTH, D], F32R)
        ids_b = sb("ids_b", [TP, IDS_RING, BATCH], I32)
        hot = sb("hot", [TP, HOT_RING, BATCH], F32R)
        hot_s = sb("hot_s", [TP, 2, BY_SCALAR, BATCH], F32R)
        distance = sb("distance", [TP, BATCH])
        zeros = sb("zeros", [P, BATCH // 2])
        dense = sb("dense", [P, BATCH])
        x_t = sb("x_t", [P, BATCH, SLOTS])
        prod = sb("prod", [P, 2, GCOLS, GROUPS])
        PW = 4 * 7 * (SLOTS + 1)
        prod_b = sb("prod_b", [P, PW])
        packed = sb("packed", [P, 2, PAIRS])
        z_t = sb("z_t", [P, KT, P])
        wd = sb("wd", [P, H1])
        wd2 = sb("wd2", [P, H1])
        wds = sb("wds", [P, H1])
        wp = sb("wp", [P, KT, H1])
        w2s = sb("w2s", [P, H1 // P, H2])
        w3s = sb("w3s", [P, H2 // P])
        b2s = sb("b2s", [P, H2 // P])
        h1 = sb("h1", [P, H1])
        h2 = sb("h2", [P, H2])
        y = sb("y", [1, BATCH])

        ps_g = [psum(f"ps_g{i}", [P, CHUNK, PITCH]) for i in range(2)]
        ps_x = [psum(f"ps_x{i}", [P, BATCH])[:] for i in range(2)]
        ps_x += [ps_g[0][:, i * (CHUNK // 2):(i + 1) * (CHUNK // 2), :].rearrange("p c n -> p (c n)") for i in range(2)]
        ps_l23 = psum("ps_l23", [P, 512])
        ps_l1 = psum("ps_l1", [P, H1])

        idx_in = sem("idx_in")
        numbers_in = sem("numbers_in")
        ident_in = sem("ident_in")
        raw_in = [sem(f"raw_in{i}") for i in range(RAW_RING)]
        ids_in = [sem(f"ids_in{i}") for i in range(IDS_RING)]
        dense_in = sem("dense_in")
        wd_in = sem("wd_in")
        wp_in = sem("wp_in")
        w2_in = sem("w2_in")
        rows_in = [[sem(f"rows_in{t}_{u}") for u in range(NU)] for t in range(TILES)]
        pad_set = sem("pad_set")
        dense_set = sem("dense_set")
        ones_set = sem("ones_set")
        wd_summed = sem("wd_summed")
        hi_ready = sem("hi_ready")
        lo_ready = sem("lo_ready")
        hot_ready = sem("hot_ready")
        hot_used = sem("hot_used")
        hot_s_ready = sem("hot_s_ready")
        distance_ready = sem("distance_ready")
        zeros_set = sem("zeros_set")
        x_ready = sem("x_ready")
        x_copied = {False: sem("x_copied_by_scalar"), True: sem("x_copied_by_vector")}
        gram_ready = sem("gram_ready")
        gram_copied = sem("gram_copied")
        turned = sem("turned")
        pairs_packed = sem("pairs_packed")
        pairs_turned = sem("pairs_turned")
        z_ready = sem("z_ready")
        l1_ready = sem("l1_ready")
        h1_ready = sem("h1_ready")
        l2_ready = sem("l2_ready")
        h2_ready = sem("h2_ready")
        l3_ready = sem("l3_ready")
        y_ready = sem("y_ready")
        out_done = sem("out_done")

        def x_places(unit):
            kind, a, u = unit
            bank = ps_x[X_INDEX[unit] % X_RING]
            if kind == "hot":
                return x_t[:, :, 1 + a], bank
            g = ROW_UNITS[u]
            return (x_t[:, a * P:(a + 1) * P, 1 + NHOT + g[0]:1 + NHOT + g[-1] + 1],
                    bank[:, 0:len(g) * P].rearrange("d (s b) -> d b s", b=P))

        NBLOCKS = len(packed_blocks())
        block = ctx.enter_context(nc.Block())

        @block.sync
        def _(sp):
            sp.dma_start(idx[:], gather_ids).then_inc(idx_in, 16)
            for j in range(NHOT):
                if j >= RAW_RING:
                    sp.wait_ge(lo_ready, j - RAW_RING + 1)
                sp.dma_start(raw[:, j % RAW_RING, 0:DEPTH[j], :],
                             tables[ONEHOT[j]].rearrange("(p k) d -> p k d", p=TP)).then_inc(raw_in[j % RAW_RING], 16)
                if j >= IDS_RING:
                    sp.wait_ge(hot_ready, HOT_BEFORE[j - IDS_RING + 1])
                    sp.wait_ge(hot_s_ready, BY_SCALAR * (j - IDS_RING + 1))
                sp.dma_start(ids_b[:, j % IDS_RING, :],
                             hot_ids[j:j + 1, :].to_broadcast([TP, BATCH])).then_inc(ids_in[j % IDS_RING], 16)
                if j == 0:
                    sp.dma_start(numbers[:], consts[0:TP, P:]).then_inc(numbers_in, 16)
                if j == 1:
                    sp.dma_start(ident_s[:], consts[:, 0:P]).then_inc(ident_in, 16)
                    sp.dma_start(dense[:], dense_t).then_inc(dense_in, 16)
                if j == NHOT - 1:
                    sp.dma_start(wd[:], w_dense).then_inc(wd_in, 16)
                    sp.dma_start(wd2[:], w_dense2).then_inc(wd_in, 16)
                    sp.dma_start(wp[0:KP, :, :], w_pairs.rearrange("(k p) n -> p k n", p=KP)).then_inc(wp_in, 16)
                    sp.dma_start(wp[KP:KP + 1, KT - 1, :], b1).then_inc(wp_in, 16)
                    sp.dma_start(w2s[:], w2.rearrange("(k p) n -> p k n", p=P)).then_inc(w2_in, 16)
                    sp.dma_start(w3s[:], w3).then_inc(w2_in, 16)
                    sp.dma_start(b2s[:], b2).then_inc(w2_in, 16)
            sp.wait_ge(y_ready, TILES)
            sp.dma_start(out, y[:]).then_inc(out_done, 16)
            sp.wait_ge(out_done, 16)

        @block.gpsimd
        def _(pool):
            pool.wait_ge(idx_in, 16)
            for t in range(TILES):
                for u in range(NU):
                    for g in ROW_UNITS[u]:
                        pool.indirect_dma_start(rows[:, t, g, :], None, tables[GATHERED[g]],
                                                bass.IndirectOffsetOnAxis(idx[:, t, g:g + 1], 0)
                                                ).then_inc(rows_in[t][u], 16)

        @block.tensor
        def _(pe):
            def x_bank(unit):
                n = X_INDEX[unit]
                grams = units_before(unit)[1]
                if n % X_RING >= 2 and grams:
                    pe.wait_ge(gram_copied, QUAD * CHUNKS * grams)
                if n >= X_RING:
                    m = n - X_RING
                    pe.wait_ge(x_copied[BY_VECTOR[m]], copies(m + 1, BY_VECTOR[m]))
                return ps_x[n % X_RING]

            def hot_rows(j):
                bank = x_bank(("hot", j, 0))
                pe.wait_ge(hi_ready, j + 1)
                pe.wait_ge(lo_ready, j + 1)
                for k in range(DEPTH[j]):
                    n, ks = HOT_BEFORE[j] + k, k - (DEPTH[j] - BY_SCALAR)
                    if ks < 0:
                        pe.wait_ge(hot_ready, n + 1)
                        one_hot = hot[:, n % HOT_RING, :]
                    else:
                        pe.wait_ge(hot_s_ready, BY_SCALAR * j + ks + 1)
                        one_hot = hot_s[:, j % 2, ks, :]
                    pe.matmul(bank, hi[:, j % SPLIT_RING, k, :], one_hot, start=(k == 0), stop=False)
                    last = pe.matmul(bank, lo[:, j % SPLIT_RING, k, :], one_hot,
                                     start=False, stop=(k == DEPTH[j] - 1))
                    if ks < 0:
                        last.then_inc(hot_used, 1)
                last.then_inc(x_ready, 1)

            def gathered_rows(t, u):
                bank = x_bank(("rows", t, u))
                pe.wait_ge(ident_in, 16)
                pe.wait_ge(rows_in[t][u], 16 * len(ROW_UNITS[u]))
                for i, g in enumerate(ROW_UNITS[u]):
                    last = pe.transpose(bank[:, i * P:(i + 1) * P], rows[:, t, g, :], ident)
                last.then_inc(x_ready, 1)

            def gram(t):
                units = units_before(("gram", t, 0))[0]
                for by_vector in (False, True):
                    if copies(units, by_vector):
                        pe.wait_ge(x_copied[by_vector], copies(units, by_vector))
                if t == 0:
                    pe.wait_ge(pad_set, 1)
                    pe.wait_ge(dense_set, 1)
                x = x_t[:, t * P:(t + 1) * P, :].rearrange("d (i q) s -> d i q s", q=QUAD)
                for c in range(CHUNKS):
                    n = t * CHUNKS + c
                    if n >= 2:
                        pe.wait_ge(gram_copied, QUAD * (n - 1))
                    for i in range(CHUNK):
                        last = pe.matmul(ps_g[n % 2][:, i, 0:QUAD * GCOLS],
                                         x[:, c * CHUNK + i, :, :].rearrange("d q s -> d (q s)"),
                                         x[:, c * CHUNK + i, :, 1:USED], start=True, stop=True)
                    last.then_inc(gram_ready, 1)

            def turn_pairs(t):
                pe.wait_ge(pairs_packed, NBLOCKS * (t + 1))
                if t >= 1:
                    pe.wait_ge(h1_ready, t)
                for k in range(KT):
                    last = pe.transpose(ps_l1[0:KP, k * P:(k + 1) * P], packed[:, t % 2, k * KP:(k + 1) * KP], ident)
                last.then_inc(pairs_turned, 1)

            def layer1(t):
                if t == 0:
                    pe.wait_ge(wd_summed, 1)
                    pe.wait_ge(wp_in, 32)
                    pe.wait_ge(ones_set, 1)
                pe.wait_ge(z_ready, t + 1)
                for n in range(H1 // P):
                    o = ps_l1[:, n * P:(n + 1) * P]
                    pe.matmul(o, wds[:, n * P:(n + 1) * P], dense[:, t * P:(t + 1) * P], start=True, stop=False)
                    for k in range(KT):
                        kp = KP + (k == KT - 1)
                        last = pe.matmul(o, wp[0:kp, k, n * P:(n + 1) * P], z_t[0:kp, k, :],
                                         start=False, stop=(k == KT - 1))
                last.then_inc(l1_ready, 1)

            def layer2(t):
                if t == 0:
                    pe.wait_ge(w2_in, 48)
                else:
                    pe.wait_ge(y_ready, t)
                pe.wait_ge(h1_ready, t + 1)
                for n in range(H2 // P):
                    for k in range(H1 // P):
                        last = pe.matmul(ps_l23[:, n * P:(n + 1) * P], w2s[:, k, n * P:(n + 1) * P],
                                         h1[:, k * P:(k + 1) * P], start=(k == 0), stop=(k == H1 // P - 1))
                last.then_inc(l2_ready, 1)

            def layer3(t):
                pe.wait_ge(h2_ready, (H2 // P) * (t + 1))
                for k in range(H2 // P):
                    last = pe.matmul(ps_l23[0:1, 384:384 + P], w3s[:, k:k + 1], h2[:, k * P:(k + 1) * P],
                                     start=(k == 0), stop=(k == H2 // P - 1))
                last.then_inc(l3_ready, 1)

            pe.wait_ge(zeros_set, 1)
            for _ in range(WARM_UP):
                pe.matmul(ps_l1[:], zeros[:].bitcast(BF16)[:, 0:P], zeros[:].bitcast(BF16), start=True, stop=True)

            for kind, a, u in STEPS:
                if kind == "hot":
                    hot_rows(a)
                elif kind == "rows":
                    gathered_rows(a, u)
                else:
                    {"gram": gram, "pairs": turn_pairs, "l1": layer1, "l2": layer2, "l3": layer3}[kind](a)

        @block.scalar
        def _(act):
            def high_part(j):
                act.wait_ge(raw_in[j % RAW_RING], 16 * (j // RAW_RING + 1))
                if j >= SPLIT_RING:
                    act.wait_ge(x_ready, X_INDEX[("hot", j - SPLIT_RING, 0)] + 1)
                act.activation(hi[:, j % SPLIT_RING, 0:DEPTH[j], :], raw[:, j % RAW_RING, 0:DEPTH[j], :],
                               ACT.Copy).then_inc(hi_ready, 1)

            def one_hot(j):
                act.wait_ge(ids_in[j % IDS_RING], 16 * (j // IDS_RING + 1))
                if j == 0:
                    act.wait_ge(numbers_in, 16)
                for ks in range(BY_SCALAR):
                    k = DEPTH[j] - BY_SCALAR + ks
                    n = BY_SCALAR * j + ks
                    if n >= 1:
                        act.wait_ge(hot_s_ready, n)
                    act.activation(distance[:], ids_b[:, j % IDS_RING, :], ACT.Abs,
                                   bias=minus_row_number[DEPTH[j]][:, k:k + 1]).then_inc(distance_ready, 1)
                    act.wait_ge(distance_ready, n + 1)
                    act.activation(hot_s[:, j % 2, ks, :], distance[:], ACT.Relu, bias=1.0,
                                   scale=-2.0).then_inc(hot_s_ready, 1)

            def copy_x(unit):
                n = X_INDEX[unit]
                if BY_VECTOR[n]:
                    return
                act.wait_ge(x_ready, n + 1)
                to, bank = x_places(unit)
                act.activation(to, bank, ACT.Copy).then_inc(x_copied[False], 1)

            def copy_gram(t):
                if t >= 2:
                    act.wait_ge(turned, t - 1)
                for c in range(CHUNKS):
                    n = t * CHUNKS + c
                    act.wait_ge(gram_ready, n + 1)
                    for q in range(QUAD):
                        p = slice(q * SLOTS, (q + 1) * SLOTS)
                        act.activation(prod[p, t % 2, :, c * CHUNK:(c + 1) * CHUNK].rearrange("p g i -> p i g"),
                                       ps_g[n % 2][p, :, q * GCOLS:(q + 1) * GCOLS], ACT.Copy
                                       ).then_inc(gram_copied, 1)

            def relu1(t):
                act.wait_ge(l1_ready, t + 1)
                if t >= 1:
                    act.wait_ge(l2_ready, t)
                act.activation(h1[:], ps_l1[:], ACT.Relu).then_inc(h1_ready, 1)

            def relu2(t):
                act.wait_ge(l2_ready, t + 1)
                if t == 0:
                    act.wait_ge(w2_in, 48)
                if t >= 1:
                    act.wait_ge(l3_ready, t)
                for n in range(H2 // P):
                    act.activation(h2[:, n * P:(n + 1) * P], ps_l23[:, n * P:(n + 1) * P], ACT.Relu,
                                   bias=b2s[:, n:n + 1]).then_inc(h2_ready, 1)

            high_part(0)
            one_hot(0)
            high_part(1)
            one_hot(1)
            for step in STEPS:
                kind, a, u = step
                if kind in ("hot", "rows"):
                    copy_x(step)
                    if kind == "hot" and a + 2 < NHOT:
                        high_part(a + 2)
                        one_hot(a + 2)
                elif kind == "gram":
                    copy_gram(a)
                elif kind == "l1":
                    relu1(a)
                elif kind == "l2":
                    relu2(a)

        @block.vector
        def _(dve):
            def low_part(j):
                dve.wait_ge(hi_ready, j + 1)
                dve.tensor_tensor(lo[:, j % SPLIT_RING, 0:DEPTH[j], :], raw[:, j % RAW_RING, 0:DEPTH[j], :],
                                  hi[:, j % SPLIT_RING, 0:DEPTH[j], :].bitcast(F32),
                                  ALU.subtract).then_inc(lo_ready, 1)

            def one_hot(j):
                dve.wait_ge(ids_in[j % IDS_RING], 16 * (j // IDS_RING + 1))
                for k in range(DEPTH[j] - BY_SCALAR):
                    n = HOT_BEFORE[j] + k
                    if n >= HOT_RING:
                        dve.wait_ge(hot_used, n - HOT_RING + 1)
                    dve.tensor_scalar(hot[:, n % HOT_RING, :], ids_b[:, j % IDS_RING, :],
                                      row_number[DEPTH[j]][:, k:k + 1], None,
                                      ALU.is_equal).then_inc(hot_ready, 1)

            def turn_gram(t):
                dve.wait_ge(gram_copied, QUAD * CHUNKS * (t + 1))
                if t >= 1:
                    dve.wait_ge(pairs_packed, NBLOCKS * t)
                dve.transpose(prod_b[:, 0:GCOLS * SLOTS], prod[:, t % 2, :, :].rearrange("p g i -> p (g i)")
                              ).then_inc(turned, 1)
                dve.wait_ge(turned, t + 1)
                if t >= 2:
                    dve.wait_ge(pairs_turned, t - 1)
                at = 0
                for (g0, gs, ng), (f0, fs, nf) in packed_blocks():
                    step = gs * SLOTS + fs
                    first = (g0 - 1) * SLOTS + f0
                    base = first // step * step if step > SLOTS else first - first % SLOTS
                    v = prod_b[:, base:base + ng * step].rearrange("p (m s) -> p m s", s=step)
                    o = packed[:, t % 2, at:at + ng * nf].rearrange("p (m s) -> p m s", s=nf)
                    dve.tensor_copy(o, v[:, :, first - base:first - base + nf]).then_inc(pairs_packed, 1)
                    at += ng * nf

            def copy_z(t):
                dve.wait_ge(pairs_turned, t + 1)
                if t >= 1:
                    dve.wait_ge(l1_ready, t)
                dve.tensor_copy(z_t[0:KP, :, :], ps_l1[0:KP, 0:KT * P].rearrange("p (k b) -> p k b", b=P)
                                ).then_inc(z_ready, 1)

            def copy_y(t):
                dve.wait_ge(l3_ready, t + 1)
                dve.tensor_copy(y[:, t * P:(t + 1) * P], ps_l23[0:1, 384:384 + P]).then_inc(y_ready, 1)

            def copy_x(unit):
                n = X_INDEX[unit]
                if not BY_VECTOR[n]:
                    return
                dve.wait_ge(x_ready, n + 1)
                to, bank = x_places(unit)
                dve.tensor_copy(to, bank).then_inc(x_copied[True], 1)

            dve.memset(zeros[:], 0.0).then_inc(zeros_set, 1)
            dve.memset(z_t[96:P, KT - 1, :], 1.0).then_inc(ones_set, 1)
            dve.memset(x_t[:, :, USED:SLOTS], 0.0).then_inc(pad_set, 1)
            dve.wait_ge(numbers_in, 16)
            dve.wait_ge(ones_set, 1)
            for j in range(NHOT):
                low_part(j)
                one_hot(j)
                if j == 0:
                    dve.wait_ge(dense_in, 16)
                    dve.tensor_copy(x_t[:, :, 0].rearrange("d (t i q) -> d t i q", t=TILES, q=QUAD),
                                    dense[:].rearrange("d (t q i) -> d t i q", t=TILES, q=QUAD)
                                    ).then_inc(dense_set, 1)
            dve.wait_ge(wd_in, 32)
            dve.tensor_tensor(wds[:], wd[:], wd2[:], ALU.add).then_inc(wd_summed, 1)
            for step in STEPS:
                kind, a, _ = step
                if kind in ("hot", "rows"):
                    copy_x(step)
                elif kind == "gram":
                    turn_gram(a)
                elif kind == "pairs":
                    copy_z(a)
                elif kind == "l3":
                    copy_y(a)


def kernel(**inputs):
    import numpy as np
    import concourse.bacc as bacc
    from concourse import mybir as mb
    from concourse.bass_utils import run_bass_kernel_spmd as run

    nc = bacc.Bacc("TRN2", target_bir_lowering=False, num_devices=1)
    ids = np.ascontiguousarray(inputs["ids"])
    w1 = np.ascontiguousarray(inputs["W_top1"])
    number = {}
    for f in range(USED):
        for g in range(f + 1, USED):
            number[f, g] = D + len(number)
    order = [number[tuple(sorted((SLOT_FEATURE[g], SLOT_FEATURE[f])))] for g, f in packed_pairs()]
    consts = np.zeros((P, P + 4 * MAXDEPTH), np.float32)
    consts[:, 0:P] = np.eye(P, dtype=np.float32)
    for i, depth in enumerate(DEPTHS):
        for p in range(TP):
            for k in range(depth):
                consts[p, P + i * MAXDEPTH + k] = p * depth + k
                consts[p, P + (i + 2) * MAXDEPTH + k] = -(p * depth + k)
    placed = ids.reshape(TILES, QUAD, GROUPS, TABLES).transpose(0, 2, 1, 3).reshape(BATCH, TABLES)
    data = {
        "gather_ids": placed[:, GATHERED].reshape(TILES, P, len(GATHERED)).transpose(1, 0, 2),
        "hot_ids": placed[:, ONEHOT].T,
        "consts": consts,
        "dense_t": np.asarray(inputs["r_dense_output"]).T,
        "w_dense": w1[0:D],
        "w_dense2": w1[D + PAIRS:],
        "w_pairs": w1[order],
        "b1": np.asarray(inputs["b_top1"]).reshape(1, H1),
        "w2": inputs["W_top2"],
        "b2": np.asarray(inputs["b_top2"]).reshape(H2 // P, P).T,
        "w3": np.asarray(inputs["W_top3"]).reshape(H2 // P, P).T,
    }
    for f in range(TABLES):
        data[f"tbl_{f}"] = inputs[f"tbl_{f}"]
    arrays, ap = {}, {}
    for name, a in data.items():
        a = np.ascontiguousarray(a)
        arrays[f"in_{name}"] = a
        ap[name] = nc.dram_tensor(f"in_{name}", a.shape, mb.dt.from_np(a.dtype), kind="ExternalInput").ap()
    o = nc.dram_tensor("out_0", (1, BATCH), mb.dt.float32, kind="ExternalOutput").ap()
    build(nc, ap["gather_ids"], ap["hot_ids"], ap["consts"], [ap[f"tbl_{f}"] for f in range(TABLES)], ap["dense_t"],
          ap["w_dense"], ap["w_dense2"], ap["w_pairs"], ap["b1"], ap["w2"], ap["b2"], ap["w3"], o)
    r = run(nc, [arrays], core_ids=[0])
    return r.results[0]["out_0"].reshape(BATCH, 1)
```

```python
from contextlib import ExitStack

import concourse.bass as bass
from concourse import mybir

F32 = mybir.dt.float32
F32R = mybir.dt.float32r
BF16 = mybir.dt.bfloat16
I32 = mybir.dt.int32
ALU = mybir.AluOpType
ACT = mybir.ActivationFunctionType

P = 128
D = 128
BATCH = 512
TILES = BATCH // P
ROWS = [1000, 12500, 1250, 1000, 125000, 1250, 12500, 1000, 1000, 1250, 1250, 12500, 1250, 1000, 12500, 1250, 1250,
        1000, 12500, 1000, 1250, 1250, 12500, 1250, 12500, 12500]
TABLES = len(ROWS)
SLOTS = 32
USED = TABLES + 1
H1, H2 = 512, 256

HOT_FROM = [(0, 0), (3, 0), (7, 0), (8, 0), (13, 0), (17, 0), (19, 0), (2, 0), (5, 3)]
ONEHOT = [f for f, _ in HOT_FROM]
FROM = [t * P for _, t in HOT_FROM]
NHOT = len(ONEHOT)
FULL = FROM.count(0)
ORDER = ONEHOT + [f for f in range(TABLES) if f not in ONEHOT]
HOT_IN = [sum(first <= t for _, first in HOT_FROM) for t in range(TILES)]
TP = 125
DEPTH = [ROWS[f] // TP for f in ONEHOT]
DEPTHS = sorted(set(DEPTH))
MAXDEPTH = max(DEPTHS)
PARTS = [[(0, d // 2), (d // 2, d)] if j == 0 else [(0, d)] for j, d in enumerate(DEPTH)]
PARTS_BEFORE = [sum(len(p) for p in PARTS[:j]) for j in range(NHOT + 1)]
BY_SCALAR = [2 if j % 3 == 1 else 1 for j in range(NHOT)]
SCALAR_BEFORE = [sum(BY_SCALAR[:j]) for j in range(NHOT + 1)]
HOT_BEFORE = [sum(DEPTH[:j]) - SCALAR_BEFORE[j] for j in range(NHOT + 1)]
SLOT_FEATURE = [0] + [1 + f for f in ORDER]

QUAD = 4
ROW_UNITS = [[range(q, min(q + QUAD, TABLES)) for q in range(HOT_IN[t], TABLES, QUAD)] for t in range(TILES)]

LAST_BY_VECTOR = 2
GROUPS = P // QUAD
CHUNK = 8
CHUNKS = GROUPS // CHUNK
PITCH = 128
GCOLS = USED - 1
GROWS = (QUAD - 1) * SLOTS + USED

PAIRS = USED * (USED - 1) // 2
KT = 3
KP = PAIRS // KT

GRAM_BANK_TILE = TILES - 2
WARM_UP = 12
RAW_RING, SPLIT_RING, IDS_RING, HOT_RING, X_RING = 3, 2, 3, 6, 4
HOT_S_RING = SPLIT_RING * max(BY_SCALAR)


def packed_blocks():
    half, b = 14, 7
    blocks = [((g0, 1, ng), (f0, 0, nf)) for g0, ng, f0, nf in
              [(half, USED - half, 0, half), (b, b, 0, b), (3 * b, USED - 3 * b, half, b)]]
    for r in range(1, b):
        m = sum(1 for i in range(4) if i * b + r < USED)
        blocks.append(((r, b, m), (0, b, r)))
    return blocks


def packed_pairs():
    return [(g0 + i * gs, f0 + i * fs + j)
            for (g0, gs, ng), (f0, fs, nf) in packed_blocks() for i in range(ng) for j in range(nf)]


def blocks_for(k):
    size = [ng * nf for (_, _, ng), (_, _, nf) in packed_blocks()]
    return min(n for n in range(len(size) + 1) if sum(size[:n]) >= (k + 1) * KP)


def schedule():
    rows = [[("rows", t, u) for u in range(len(ROW_UNITS[t]))] for t in range(TILES)]
    gram = [[("gram", t, c) for c in range(CHUNKS)] for t in range(TILES)]
    early = rows[0] + rows[1]
    steps = [("hot", 0, 0)]
    for j in range(1, FULL):
        steps += [("hot", j, 0)] + early[j - 1:j] * (j < FULL - 1)
    steps += early[FULL - 2:FULL]
    late = [("hot", j, 0) for j in range(FULL, NHOT)]
    for step in (late, gram[0][0:2], early[FULL:FULL + 1], gram[0][2:3], early[FULL + 1:], gram[0][3:4],
                 "turn 0", gram[1], "pairs 0", "turn 1", "dense 0", "l1 0", "pairs 1", rows[2][:2], "l2 0", "dense 1",
                 rows[2][2:], "l1 1", "l3 0", gram[2], "turn 2", "l2 1", rows[3][:3], "pairs 2", rows[3][3:4], "l3 1",
                 rows[3][4:], "dense 2", gram[3], "turn 3", "l1 2", "pairs 3", "dense 3", "l1 3", "l2 2", "l2 3",
                 "l3 2", "l3 3"):
        if isinstance(step, str):
            kind, t = step.split()
            step = [(kind, int(t), 0)]
        steps += step
    return steps


STEPS = schedule()
X_UNITS = [s for s in STEPS if s[0] in ("hot", "rows", "pairs")]
X_INDEX = {s: n for n, s in enumerate(X_UNITS)}


def banks():
    at, run = [], 0
    for kind, _, _ in STEPS + [("gram", TILES, 0)]:
        if kind == "gram":
            at += [(n - run + 2) % X_RING for n in range(run)]
            run = 0
        elif kind in ("hot", "rows", "pairs"):
            run += 1
    return at


X_BANK = banks()
BY_VECTOR = [s[0] == "pairs" or (s[0] == "rows" and n > X_INDEX[("hot", NHOT - 1, 0)] + 1 and s[2] % 2 == 1)
             for n, s in enumerate(X_UNITS)]


def copies(n, by_vector):
    return BY_VECTOR[:n].count(by_vector)


def copied_by(chunks, by_vector):
    return chunks // CHUNKS * LAST_BY_VECTOR if by_vector else chunks * QUAD - chunks // CHUNKS * LAST_BY_VECTOR


def in_gram_bank(before):
    chunks = [n for n, s in enumerate(s for s in STEPS if s[0] == "gram") if s in STEPS[:before] and n % 2 == 0]
    return chunks[-1] + 1 if chunks else 0


def units_for(t, c):
    before = STEPS[:STEPS.index(("gram", t, c))]
    done = {n: s for n, s in enumerate(X_UNITS) if s in before}
    own = [n for n, s in done.items() if s[:2] == ("rows", t) or (s[0] == "hot" and FROM[s[1]] <= t * P)]
    in_bank = [n for n in done if X_BANK[n] >= 2]
    return 1 + max([-1] + own * (c == 0) + in_bank * (c % 2 == 0))


def build(nc, gather_ids, hot_ids, consts, tables, dense_t, w_dense, w_dense2, w_pairs, b1, w2, b2, w3, out):
    with ExitStack() as ctx:
        def sb(name, shape, dt=F32):
            return ctx.enter_context(nc.sbuf_tensor(name, shape, dt))

        def psum(name, shape, dt=F32):
            return ctx.enter_context(nc.psum_tensor(name, shape, dt))

        def sem(name):
            return ctx.enter_context(nc.semaphore(name))

        idx = sb("idx", [P, TILES, TABLES], I32)
        ident_s = sb("ident", [P, P])
        ident = ident_s[:]
        numbers = sb("numbers", [TP, 4 * MAXDEPTH])
        row_number, minus_row_number = [
            {d: numbers[:, (i + s) * MAXDEPTH:(i + s + 1) * MAXDEPTH] for i, d in enumerate(DEPTHS)} for s in (0, 2)]
        rows = sb("rows", [P, TILES, TABLES - HOT_IN[0], D])
        raw = sb("raw", [TP, RAW_RING, MAXDEPTH, D])
        hi = sb("hi", [TP, SPLIT_RING, MAXDEPTH, D], F32R)
        lo = sb("lo", [TP, SPLIT_RING, MAXDEPTH, D], F32R)
        ids_b = sb("ids_b", [TP, IDS_RING, BATCH], I32)
        hot = sb("hot", [TP, HOT_RING, BATCH], F32R)
        hot_s = sb("hot_s", [TP, HOT_S_RING, BATCH], F32R)
        distance = sb("distance", [TP, BATCH])
        zeros = sb("zeros", [P, BATCH // 2])
        dense = sb("dense", [P, BATCH])
        x_t = sb("x_t", [P, BATCH, SLOTS])
        prod = sb("prod", [P, 2, GCOLS, GROUPS])
        prod_b = sb("prod_b", [P, 4 * 7 * (SLOTS + 1)])
        packed = sb("packed", [P, 2, PAIRS])
        z_t = sb("z_t", [P, 2, KT, P])
        wd = sb("wd", [P, H1])
        wd2 = sb("wd2", [P, H1])
        wds = sb("wds", [P, H1])
        wp = sb("wp", [P, KT, H1])
        w2s = sb("w2s", [P, H1 // P, H2])
        w3s = sb("w3s", [P, H2 // P])
        b2s = sb("b2s", [P, H2 // P])
        h1 = sb("h1", [P, 2, H1])
        h2 = sb("h2", [P, 2, H2])
        y = sb("y", [1, BATCH])

        ps_g = [psum(f"ps_g{i}", [P, CHUNK, PITCH]) for i in range(2)]
        ps_x = [psum(f"ps_x{i}", [P, BATCH])[:] for i in range(2)]
        ps_x += [ps_g[0][:, i * (CHUNK // 2):(i + 1) * (CHUNK // 2), :].rearrange("p c n -> p (c n)") for i in range(2)]
        ps_l1 = psum("ps_l1", [P, H1])
        ps_l23 = psum("ps_l23", [P, 2 * H2])
        ps_l23 = [ps_x[2] if t == GRAM_BANK_TILE else ps_l23[:] for t in range(TILES)]
        ps_l2 = [[ps_x[3] if t == TILES - 1 and n else ps_l23[t] for n in range(H2 // P)] for t in range(TILES)]

        idx_in = sem("idx_in")
        numbers_in = sem("numbers_in")
        ident_in = sem("ident_in")
        raw_in = [[sem(f"raw_in{r}_{i}") for i in range(max(len(p) for p in PARTS[r::RAW_RING]))]
                  for r in range(RAW_RING)]
        ids_in = [sem(f"ids_in{i}") for i in range(IDS_RING)]
        dense_in = sem("dense_in")
        wd_in = sem("wd_in")
        wp_in = sem("wp_in")
        w2_in = sem("w2_in")
        rows_in = [[sem(f"rows_in{t}_{u}") for u in range(len(ROW_UNITS[t]))] for t in range(TILES)]
        pad_set = sem("pad_set")
        dense_set = sem("dense_set")
        ones_set = sem("ones_set")
        prod_set = sem("prod_set")
        wd_summed = sem("wd_summed")
        hi_ready = sem("hi_ready")
        lo_ready = sem("lo_ready")
        hot_ready = sem("hot_ready")
        hot_used = sem("hot_used")
        hot_s_ready = sem("hot_s_ready")
        distance_ready = sem("distance_ready")
        zeros_set = sem("zeros_set")
        x_ready = sem("x_ready")
        x_copied = {False: sem("x_copied_by_scalar"), True: sem("x_copied_by_vector")}
        gram_ready = sem("gram_ready")
        gram_copied = {False: sem("gram_copied_by_scalar"), True: sem("gram_copied_by_vector")}
        turned = sem("turned")
        pairs_packed = sem("pairs_packed")
        l1_ready = sem("l1_ready")
        h1_ready = sem("h1_ready")
        l2_ready = sem("l2_ready")
        h2_ready = sem("h2_ready")
        l3_ready = sem("l3_ready")
        y_ready = sem("y_ready")
        out_done = sem("out_done")

        def x_places(unit):
            kind, a, u = unit
            bank = ps_x[X_BANK[X_INDEX[unit]]]
            if kind == "hot":
                return x_t[:, FROM[a]:, 1 + a], bank[:, FROM[a]:]
            g = ROW_UNITS[a][u]
            return (x_t[:, a * P:(a + 1) * P, 1 + g[0]:1 + g[-1] + 1],
                    bank[:, 0:len(g) * P].rearrange("d (s b) -> d b s", b=P))

        def gram_places(n, q):
            t, c = divmod(n, CHUNKS)
            p = slice(q * SLOTS, min((q + 1) * SLOTS, GROWS))
            return (prod[p, t % 2, :, c * CHUNK:(c + 1) * CHUNK].rearrange("p g i -> p i g"),
                    ps_g[n % 2][p, :, q * GCOLS:(q + 1) * GCOLS])

        NBLOCKS = len(packed_blocks())
        block = ctx.enter_context(nc.Block())

        @block.sync
        def _(sp):
            sp.dma_start(idx[:], gather_ids).then_inc(idx_in, 16)

            def load_table(j):
                if j >= RAW_RING:
                    sp.wait_ge(lo_ready, PARTS_BEFORE[j - RAW_RING + 1])
                for i, (a, b) in enumerate(PARTS[j]):
                    sp.dma_start(raw[:, j % RAW_RING, a:b, :],
                                 tables[ONEHOT[j]].rearrange("(p k) d -> p k d", p=TP)[:, a:b, :]
                                 ).then_inc(raw_in[j % RAW_RING][i], 16)

            def load_ids(j):
                if j >= IDS_RING:
                    sp.wait_ge(hot_ready, HOT_BEFORE[j - IDS_RING + 1])
                    sp.wait_ge(hot_s_ready, SCALAR_BEFORE[j - IDS_RING + 1])
                sp.dma_start(ids_b[:, j % IDS_RING, :],
                             hot_ids[j:j + 1, :].to_broadcast([TP, BATCH])).then_inc(ids_in[j % IDS_RING], 16)

            load_ids(0)
            sp.dma_start(numbers[:], consts[0:TP, P:]).then_inc(numbers_in, 16)
            load_table(0)
            for j in range(1, NHOT):
                load_table(j)
                load_ids(j)
                if j == 1:
                    sp.dma_start(ident_s[:], consts[:, 0:P]).then_inc(ident_in, 16)
                    sp.dma_start(dense[:], dense_t).then_inc(dense_in, 16)
                if j == NHOT - 1:
                    sp.dma_start(wd[:], w_dense).then_inc(wd_in, 16)
                    sp.dma_start(wd2[:], w_dense2).then_inc(wd_in, 16)
                    sp.dma_start(wp[0:KP, :, :], w_pairs.rearrange("(k p) n -> p k n", p=KP)).then_inc(wp_in, 16)
                    sp.dma_start(wp[KP:KP + 1, KT - 1, :], b1).then_inc(wp_in, 16)
                    sp.dma_start(w2s[:], w2.rearrange("(k p) n -> p k n", p=P)).then_inc(w2_in, 16)
                    sp.dma_start(w3s[:], w3).then_inc(w2_in, 16)
                    sp.dma_start(b2s[:], b2).then_inc(w2_in, 16)
            sp.wait_ge(y_ready, TILES)
            sp.dma_start(out, y[:]).then_inc(out_done, 16)
            sp.wait_ge(out_done, 16)

        @block.gpsimd
        def _(pool):
            pool.wait_ge(idx_in, 16)
            for t in range(TILES):
                for u, unit in enumerate(ROW_UNITS[t]):
                    for g in unit:
                        pool.indirect_dma_start(rows[:, t, g - HOT_IN[0], :], None, tables[ORDER[g]],
                                                bass.IndirectOffsetOnAxis(idx[:, t, g:g + 1], 0)
                                                ).then_inc(rows_in[t][u], 16)

        @block.tensor
        def _(pe):
            def x_bank(unit):
                n = X_INDEX[unit]
                chunks = in_gram_bank(STEPS.index(unit))
                if X_BANK[n] >= 2 and chunks:
                    pe.wait_ge(gram_copied[False], copied_by(chunks, False))
                if X_BANK[n] in X_BANK[:n]:
                    m = max(m for m in range(n) if X_BANK[m] == X_BANK[n])
                    pe.wait_ge(x_copied[BY_VECTOR[m]], copies(m + 1, BY_VECTOR[m]))
                return ps_x[X_BANK[n]]

            def hot_rows(j):
                bank = x_bank(("hot", j, 0))
                for k in range(DEPTH[j]):
                    for i, (a, b) in enumerate(PARTS[j]):
                        if k == a:
                            pe.wait_ge(hi_ready, PARTS_BEFORE[j] + i + 1)
                            pe.wait_ge(lo_ready, PARTS_BEFORE[j] + i + 1)
                    n, ks = HOT_BEFORE[j] + k, k - (DEPTH[j] - BY_SCALAR[j])
                    if ks < 0:
                        pe.wait_ge(hot_ready, n + 1)
                        one_hot = hot[:, n % HOT_RING, :]
                    else:
                        pe.wait_ge(hot_s_ready, SCALAR_BEFORE[j] + ks + 1)
                        one_hot = hot_s[:, (SCALAR_BEFORE[j] + ks) % HOT_S_RING, :]
                    pe.matmul(bank[:, FROM[j]:], hi[:, j % SPLIT_RING, k, :], one_hot[:, FROM[j]:],
                              start=(k == 0), stop=False)
                    last = pe.matmul(bank[:, FROM[j]:], lo[:, j % SPLIT_RING, k, :], one_hot[:, FROM[j]:],
                                     start=False, stop=(k == DEPTH[j] - 1))
                    if ks < 0:
                        last.then_inc(hot_used, 1)
                last.then_inc(x_ready, 1)

            def gathered_rows(t, u):
                bank = x_bank(("rows", t, u))
                pe.wait_ge(ident_in, 16)
                pe.wait_ge(rows_in[t][u], 16 * len(ROW_UNITS[t][u]))
                for i, g in enumerate(ROW_UNITS[t][u]):
                    last = pe.transpose(bank[:, i * P:(i + 1) * P], rows[:, t, g - HOT_IN[0], :], ident)
                last.then_inc(x_ready, 1)

            def gram(t, c):
                units = units_for(t, c)
                for by_vector in (False, True):
                    if copies(units, by_vector):
                        pe.wait_ge(x_copied[by_vector], copies(units, by_vector))
                if t == 0 and c == 0:
                    pe.wait_ge(pad_set, 1)
                    pe.wait_ge(dense_set, 1)
                x = x_t[:, t * P:(t + 1) * P, :].rearrange("d (i q) s -> d i q s", q=QUAD)
                n = t * CHUNKS + c
                if n >= 2:
                    pe.wait_ge(gram_copied[False], copied_by(n - 1, False))
                    if n % CHUNKS == 1:
                        pe.wait_ge(gram_copied[True], copied_by(n - 1, True))
                for i in range(CHUNK):
                    last = pe.matmul(ps_g[n % 2][0:GROWS, i, 0:QUAD * GCOLS],
                                     x[:, c * CHUNK + i, :, :].rearrange("d q s -> d (q s)")[:, 0:GROWS],
                                     x[:, c * CHUNK + i, :, 1:USED], start=True, stop=True)
                last.then_inc(gram_ready, 1)

            def turn_pairs(t):
                bank = x_bank(("pairs", t, 0))
                for k in range(KT):
                    pe.wait_ge(pairs_packed, NBLOCKS * t + blocks_for(k))
                    last = pe.transpose(bank[0:KP, k * P:(k + 1) * P], packed[:, t % 2, k * KP:(k + 1) * KP], ident)
                last.then_inc(x_ready, 1)

            def layer1_dense(t):
                if t == 0:
                    pe.wait_ge(wd_summed, 1)
                else:
                    pe.wait_ge(h1_ready, t)
                for n in range(H1 // P):
                    pe.matmul(ps_l1[:, n * P:(n + 1) * P], wds[:, n * P:(n + 1) * P], dense[:, t * P:(t + 1) * P],
                              start=(n == 0), stop=False, skip_group_check=True)

            def layer1(t):
                if t == 0:
                    pe.wait_ge(wp_in, 32)
                    pe.wait_ge(ones_set, 1)
                pe.wait_ge(x_copied[True], copies(X_INDEX[("pairs", t, 0)] + 1, True))
                for k in range(KT):
                    kp = KP + (k == KT - 1)
                    for n in range(H1 // P):
                        last = pe.matmul(ps_l1[:, n * P:(n + 1) * P], wp[0:kp, k, n * P:(n + 1) * P],
                                         z_t[0:kp, t % 2, k, :], start=False, stop=(k == KT - 1),
                                         skip_group_check=True)
                last.then_inc(l1_ready, 1)

            def layer2(t):
                if t == 0:
                    pe.wait_ge(w2_in, 48)
                elif t == GRAM_BANK_TILE:
                    pe.wait_ge(gram_copied[False], copied_by(CHUNKS * TILES - 1, False))
                else:
                    pe.wait_ge(y_ready, t - 1 if t - 1 == GRAM_BANK_TILE else t)
                pe.wait_ge(h1_ready, t + 1)
                for n in range(H2 // P):
                    for k in range(H1 // P):
                        last = pe.matmul(ps_l2[t][n][:, n * P:(n + 1) * P], w2s[:, k, n * P:(n + 1) * P],
                                         h1[:, t % 2, k * P:(k + 1) * P], start=(k == 0), stop=(k == H1 // P - 1))
                    last.then_inc(l2_ready, 1)

            def layer3(t):
                for k in range(H2 // P):
                    pe.wait_ge(h2_ready, (H2 // P) * t + (k + 1 if t == TILES - 1 else H2 // P))
                    last = pe.matmul(ps_l23[t][0:1, 384:384 + P], w3s[:, k:k + 1], h2[:, t % 2, k * P:(k + 1) * P],
                                     start=(k == 0), stop=(k == H2 // P - 1))
                last.then_inc(l3_ready, 1)

            pe.wait_ge(zeros_set, 1)
            for _ in range(WARM_UP):
                pe.matmul(ps_l1[:], zeros[:].bitcast(BF16)[:, 0:P], zeros[:].bitcast(BF16), start=True, stop=True)

            for kind, a, u in STEPS:
                if kind == "hot":
                    hot_rows(a)
                elif kind == "rows":
                    gathered_rows(a, u)
                elif kind == "gram":
                    gram(a, u)
                elif kind != "turn":
                    {"pairs": turn_pairs, "dense": layer1_dense, "l1": layer1, "l2": layer2, "l3": layer3}[kind](a)

        @block.scalar
        def _(act):
            def high_part(j):
                if j >= SPLIT_RING:
                    act.wait_ge(x_ready, X_INDEX[("hot", j - SPLIT_RING, 0)] + 1)
                for i, (a, b) in enumerate(PARTS[j]):
                    act.wait_ge(raw_in[j % RAW_RING][i], 16 * len([m for m in range(j % RAW_RING, j + 1, RAW_RING)
                                                                     if i < len(PARTS[m])]))
                    act.activation(hi[:, j % SPLIT_RING, a:b, :], raw[:, j % RAW_RING, a:b, :],
                                   ACT.Copy).then_inc(hi_ready, 1)

            def one_hot(j):
                act.wait_ge(ids_in[j % IDS_RING], 16 * (j // IDS_RING + 1))
                if j == 0:
                    act.wait_ge(numbers_in, 16)
                for ks in range(BY_SCALAR[j]):
                    k = DEPTH[j] - BY_SCALAR[j] + ks
                    n = SCALAR_BEFORE[j] + ks
                    if n >= 1:
                        act.wait_ge(hot_s_ready, n)
                    act.activation(distance[:, FROM[j]:], ids_b[:, j % IDS_RING, FROM[j]:], ACT.Abs,
                                   bias=minus_row_number[DEPTH[j]][:, k:k + 1]).then_inc(distance_ready, 1)
                    act.wait_ge(distance_ready, n + 1)
                    act.activation(hot_s[:, n % HOT_S_RING, FROM[j]:], distance[:, FROM[j]:], ACT.Relu, bias=1.0,
                                   scale=-2.0).then_inc(hot_s_ready, 1)

            def copy_x(unit):
                n = X_INDEX[unit]
                if BY_VECTOR[n]:
                    return
                act.wait_ge(x_ready, n + 1)
                to, bank = x_places(unit)
                act.activation(to, bank, ACT.Copy).then_inc(x_copied[False], 1)

            def copy_gram(t, c):
                if t >= 2 and c == 0:
                    act.wait_ge(turned, t - 1)
                n = t * CHUNKS + c
                if n == 0:
                    act.wait_ge(prod_set, 1)
                act.wait_ge(gram_ready, n + 1)
                for q in range(QUAD - LAST_BY_VECTOR if c == CHUNKS - 1 else QUAD):
                    to, block = gram_places(n, q)
                    act.activation(to, block, ACT.Copy).then_inc(gram_copied[False], 1)

            def relu1(t):
                act.wait_ge(l1_ready, t + 1)
                if t >= 2:
                    act.wait_ge(l2_ready, (H2 // P) * (t - 1))
                act.activation(h1[:, t % 2, :], ps_l1[:], ACT.Relu).then_inc(h1_ready, 1)

            def relu2(t):
                if t == 0:
                    act.wait_ge(w2_in, 48)
                if t >= 2:
                    act.wait_ge(l3_ready, t - 1)
                for n in range(H2 // P):
                    act.wait_ge(l2_ready, (H2 // P) * t + (n + 1 if t == TILES - 1 else H2 // P))
                    act.activation(h2[:, t % 2, n * P:(n + 1) * P], ps_l2[t][n][:, n * P:(n + 1) * P], ACT.Relu,
                                   bias=b2s[:, n:n + 1]).then_inc(h2_ready, 1)

            high_part(0)
            one_hot(0)
            high_part(1)
            one_hot(1)
            for step in STEPS:
                kind, a, u = step
                if kind in ("hot", "rows"):
                    copy_x(step)
                    if kind == "hot" and a + 2 < NHOT:
                        high_part(a + 2)
                        one_hot(a + 2)
                elif kind == "gram":
                    copy_gram(a, u)
                elif kind == "l1":
                    relu1(a)
                elif kind == "l2":
                    relu2(a)

        @block.vector
        def _(dve):
            def low_part(j, i):
                a, b = PARTS[j][i]
                dve.wait_ge(hi_ready, PARTS_BEFORE[j] + i + 1)
                dve.tensor_tensor(lo[:, j % SPLIT_RING, a:b, :], raw[:, j % RAW_RING, a:b, :],
                                  hi[:, j % SPLIT_RING, a:b, :].bitcast(F32), ALU.subtract).then_inc(lo_ready, 1)

            def one_hot(j, a, b):
                dve.wait_ge(ids_in[j % IDS_RING], 16 * (j // IDS_RING + 1))
                for k in range(a, b):
                    n = HOT_BEFORE[j] + k
                    if n >= HOT_RING:
                        dve.wait_ge(hot_used, n - HOT_RING + 1)
                    dve.tensor_scalar(hot[:, n % HOT_RING, FROM[j]:], ids_b[:, j % IDS_RING, FROM[j]:],
                                      row_number[DEPTH[j]][:, k:k + 1], None,
                                      ALU.is_equal).then_inc(hot_ready, 1)

            def turn_gram(t):
                n = CHUNKS * (t + 1)
                dve.wait_ge(gram_ready, n)
                if t == 0:
                    dve.wait_ge(prod_set, 1)
                for q in range(QUAD - LAST_BY_VECTOR, QUAD):
                    to, block = gram_places(n - 1, q)
                    dve.tensor_copy(to, block).then_inc(gram_copied[True], 1)
                for by_vector in (False, True):
                    dve.wait_ge(gram_copied[by_vector], copied_by(n, by_vector))
                if t >= 1:
                    dve.wait_ge(pairs_packed, NBLOCKS * t)
                dve.transpose(prod_b[:, 0:GCOLS * SLOTS], prod[:, t % 2, :, :].rearrange("p g i -> p (g i)")
                              ).then_inc(turned, 1)
                dve.wait_ge(turned, t + 1)
                if t >= 2:
                    dve.wait_ge(x_ready, X_INDEX[("pairs", t - 2, 0)] + 1)
                at = 0
                for (g0, gs, ng), (f0, fs, nf) in packed_blocks():
                    step = gs * SLOTS + fs
                    first = (g0 - 1) * SLOTS + f0
                    base = first // step * step if step > SLOTS else first - first % SLOTS
                    v = prod_b[:, base:base + ng * step].rearrange("p (m s) -> p m s", s=step)
                    o = packed[:, t % 2, at:at + ng * nf].rearrange("p (m s) -> p m s", s=nf)
                    dve.tensor_copy(o, v[:, :, first - base:first - base + nf]).then_inc(pairs_packed, 1)
                    at += ng * nf

            def copy_z(t):
                n = X_INDEX[("pairs", t, 0)]
                dve.wait_ge(x_ready, n + 1)
                if t == 0:
                    dve.wait_ge(ones_set, 1)
                if t >= 2:
                    dve.wait_ge(l1_ready, t - 1)
                dve.tensor_copy(z_t[0:KP, t % 2, :, :],
                                ps_x[X_BANK[n]][0:KP, 0:KT * P].rearrange("p (k b) -> p k b", b=P)
                                ).then_inc(x_copied[True], 1)

            def copy_y(t):
                dve.wait_ge(l3_ready, t + 1)
                dve.tensor_copy(y[:, t * P:(t + 1) * P], ps_l23[t][0:1, 384:384 + P]).then_inc(y_ready, 1)

            def copy_x(unit):
                n = X_INDEX[unit]
                if not BY_VECTOR[n]:
                    return
                dve.wait_ge(x_ready, n + 1)
                to, bank = x_places(unit)
                dve.tensor_copy(to, bank).then_inc(x_copied[True], 1)

            dve.memset(zeros[:], 0.0).then_inc(zeros_set, 1)
            dve.memset(x_t[:, :, USED:SLOTS], 0.0).then_inc(pad_set, 1)
            dve.wait_ge(numbers_in, 16)
            one_hot(0, 0, 3)
            low_part(0, 0)
            one_hot(0, 3, 4)
            low_part(0, 1)
            one_hot(0, 4, DEPTH[0] - BY_SCALAR[0])
            for j in range(1, NHOT):
                low_part(j, 0)
                one_hot(j, 0, DEPTH[j] - BY_SCALAR[j])
            dve.wait_ge(dense_in, 16)
            dve.tensor_copy(x_t[:, :, 0].rearrange("d (t i q) -> d t i q", t=TILES, q=QUAD),
                            dense[:].rearrange("d (t q i) -> d t i q", t=TILES, q=QUAD)).then_inc(dense_set, 1)
            dve.memset(prod[96:P, :, :, :], 0.0).then_inc(prod_set, 1)
            dve.memset(z_t[96:P, :, KT - 1, :], 1.0).then_inc(ones_set, 1)
            dve.wait_ge(wd_in, 32)
            dve.tensor_tensor(wds[:], wd[:], wd2[:], ALU.add).then_inc(wd_summed, 1)
            for step in STEPS:
                kind, a, _ = step
                if kind in ("hot", "rows"):
                    copy_x(step)
                elif kind == "turn":
                    turn_gram(a)
                elif kind == "pairs":
                    copy_z(a)
                elif kind == "l3":
                    copy_y(a)


def kernel(**inputs):
    import numpy as np
    import concourse.bacc as bacc
    from concourse import mybir as mb
    from concourse.bass_utils import run_bass_kernel_spmd as run

    nc = bacc.Bacc("TRN2", target_bir_lowering=False, num_devices=1)
    ids = np.ascontiguousarray(inputs["ids"])
    w1 = np.ascontiguousarray(inputs["W_top1"])
    number = {}
    for f in range(USED):
        for g in range(f + 1, USED):
            number[f, g] = D + len(number)
    order = [number[tuple(sorted((SLOT_FEATURE[g], SLOT_FEATURE[f])))] for g, f in packed_pairs()]
    consts = np.zeros((P, P + 4 * MAXDEPTH), np.float32)
    consts[:, 0:P] = np.eye(P, dtype=np.float32)
    for i, depth in enumerate(DEPTHS):
        for p in range(TP):
            for k in range(depth):
                consts[p, P + i * MAXDEPTH + k] = p * depth + k
                consts[p, P + (i + 2) * MAXDEPTH + k] = -(p * depth + k)
    placed = ids.reshape(TILES, QUAD, GROUPS, TABLES).transpose(0, 2, 1, 3).reshape(BATCH, TABLES)
    data = {
        "gather_ids": placed[:, ORDER].reshape(TILES, P, TABLES).transpose(1, 0, 2),
        "hot_ids": placed[:, ONEHOT].T,
        "consts": consts,
        "dense_t": np.asarray(inputs["r_dense_output"]).T,
        "w_dense": w1[0:D],
        "w_dense2": w1[D + PAIRS:],
        "w_pairs": w1[order],
        "b1": np.asarray(inputs["b_top1"]).reshape(1, H1),
        "w2": inputs["W_top2"],
        "b2": np.asarray(inputs["b_top2"]).reshape(H2 // P, P).T,
        "w3": np.asarray(inputs["W_top3"]).reshape(H2 // P, P).T,
    }
    for f in range(TABLES):
        data[f"tbl_{f}"] = inputs[f"tbl_{f}"]
    arrays, ap = {}, {}
    for name, a in data.items():
        a = np.ascontiguousarray(a)
        arrays[f"in_{name}"] = a
        ap[name] = nc.dram_tensor(f"in_{name}", a.shape, mb.dt.from_np(a.dtype), kind="ExternalInput").ap()
    o = nc.dram_tensor("out_0", (1, BATCH), mb.dt.float32, kind="ExternalOutput").ap()
    build(nc, ap["gather_ids"], ap["hot_ids"], ap["consts"], [ap[f"tbl_{f}"] for f in range(TABLES)], ap["dense_t"],
          ap["w_dense"], ap["w_dense2"], ap["w_pairs"], ap["b1"], ap["w2"], ap["b2"], ap["w3"], o)
    r = run(nc, [arrays], core_ids=[0])
    return r.results[0]["out_0"].reshape(BATCH, 1)
```
